# Optimizing a Trainium2 kernel written in Bass

```python
import numpy as np
import jax
import jax.numpy as jnp

def _softmax(x, axis=-1):
    return jax.nn.softmax(x, axis=axis)

def _gelu(x):
    return jax.nn.gelu(x, approximate=True)

def _silu(x):
    return jax.nn.silu(x)

def _sigmoid(x):
    return jax.nn.sigmoid(x)

def _layernorm(x, axis=-1, eps=1e-05):
    m = jnp.mean(x, axis=axis, keepdims=True)
    v = jnp.var(x, axis=axis, keepdims=True)
    return (x - m) / jnp.sqrt(v + eps)

def _scatter_add(tgt, idx, src, axis=0):
    return tgt.at[idx].add(src)

def _segment_sum(src, seg, n):
    return jax.ops.segment_sum(src, seg, n)
kernel_name = 'mk_seq_postln_d1_jaxref_r8_698a29'

def setup_inputs(seed: int=0):
    np.random.seed(seed)
    _w = jnp.asarray

    def _L0_attn_setup():
        import jax, jax.numpy as jnp
        import numpy as np
        B, L = (4, 256)
        D_MODEL, D_INNER, D_STATE, DT_RANK, D_CONV = (128, 256, 16, 64, 4)
        key = jax.random.key(seed)
        ks = jax.random.split(key, 10)
        s = lambda k, shape, sc: jax.random.normal(k, shape, dtype=jnp.float32) * sc
        return {'x': s(ks[0], (B, L, D_MODEL), 1.0), 'W_in': s(ks[1], (2 * D_INNER, D_MODEL), D_MODEL ** (-0.5)), 'conv_w': s(ks[2], (D_INNER, D_CONV), D_CONV ** (-0.5)), 'conv_b': s(ks[3], (D_INNER,), 0.02), 'A_log': jnp.log(jnp.arange(1, D_STATE + 1, dtype=jnp.float32)), 'D': jnp.ones((D_INNER,), dtype=jnp.float32), 'W_x': s(ks[4], (DT_RANK + 2 * D_STATE, D_INNER), D_INNER ** (-0.5)), 'W_dt': s(ks[5], (D_INNER, DT_RANK), DT_RANK ** (-0.5)), 'b_dt': s(ks[6], (D_INNER,), 0.02) - 4.0, 'W_out': s(ks[7], (D_MODEL, D_INNER), D_INNER ** (-0.5))}
    _L0_attn_in = _L0_attn_setup()

    def _L0_ffn_setup():
        import jax, jax.numpy as jnp
        import numpy as np
        E = 8
        K = 2
        D = 128
        P = 512
        key = jax.random.key(seed)
        ks = jax.random.split(key, 8)
        s = lambda fan_in: 1.0 / np.sqrt(fan_in)
        x = jax.random.normal(ks[0], (2, 256, D), dtype=jnp.float32)
        W1 = jax.random.normal(ks[1], (E, D, P), dtype=jnp.float32) * s(D)
        b1 = jax.random.normal(ks[2], (E, P), dtype=jnp.float32) * 0.01
        W2 = jax.random.normal(ks[3], (E, P, D), dtype=jnp.float32) * s(P)
        b2 = jax.random.normal(ks[4], (E, D), dtype=jnp.float32) * 0.01
        Wr = jax.random.normal(ks[5], (D, E), dtype=jnp.float32) * s(D)
        br = jax.random.normal(ks[6], (E,), dtype=jnp.float32) * 0.01
        return {'x': x, 'W1': W1, 'b1': b1, 'W2': W2, 'b2': b2, 'Wr': Wr, 'br': br}
    _L0_ffn_in = _L0_ffn_setup()
    _d = {'L0_attn_x': _L0_attn_in['x'], 'L0_attn_W_in': _L0_attn_in['W_in'], 'L0_attn_conv_w': _L0_attn_in['conv_w'], 'L0_attn_conv_b': _L0_attn_in['conv_b'], 'L0_attn_A_log': _L0_attn_in['A_log'], 'L0_attn_D': _L0_attn_in['D'], 'L0_attn_W_x': _L0_attn_in['W_x'], 'L0_attn_W_dt': _L0_attn_in['W_dt'], 'L0_attn_b_dt': _L0_attn_in['b_dt'], 'L0_attn_W_out': _L0_attn_in['W_out'], 'L0_ffn_W1': _L0_ffn_in['W1'], 'L0_ffn_b1': _L0_ffn_in['b1'], 'L0_ffn_W2': _L0_ffn_in['W2'], 'L0_ffn_b2': _L0_ffn_in['b2'], 'L0_ffn_Wr': _L0_ffn_in['Wr'], 'L0_ffn_br': _L0_ffn_in['br']}
    _x0 = _d['L0_attn_x']
    _d['L0_attn_x'] = jax.random.normal(jax.random.fold_in(jax.random.key(seed), 1), (4, 1024, 128), dtype=_x0.dtype)
    del _x0
    return _d

def reference(L0_attn_x, L0_attn_W_in, L0_attn_conv_w, L0_attn_conv_b, L0_attn_A_log, L0_attn_D, L0_attn_W_x, L0_attn_W_dt, L0_attn_b_dt, L0_attn_W_out, L0_ffn_W1, L0_ffn_b1, L0_ffn_W2, L0_ffn_b2, L0_ffn_Wr, L0_ffn_br):

    def _L0_attn_ref(x, W_in, conv_w, conv_b, A_log, D, W_x, W_dt, b_dt, W_out):
        import jax, jax.numpy as jnp
        import numpy as np
        B, L = (4, 256)
        D_MODEL, D_INNER, D_STATE, DT_RANK, D_CONV = (128, 256, 16, 64, 4)
        Bb, Ll, _ = x.shape
        xz = x @ W_in.T
        xr, z = jnp.split(xz, 2, axis=-1)
        xc = jax.lax.conv_general_dilated(xr.transpose(0, 2, 1), conv_w[:, None, :], window_strides=(1,), padding=[(D_CONV - 1, 0)], dimension_numbers=('NCH', 'OIH', 'NCH'), feature_group_count=D_INNER) + conv_b[None, :, None]
        xs = jax.nn.silu(xc.transpose(0, 2, 1))
        x_dbl = xs @ W_x.T
        dt_r, b_sel, c_sel = jnp.split(x_dbl, [DT_RANK, DT_RANK + D_STATE], axis=-1)
        dt = jax.nn.softplus(dt_r @ W_dt.T + b_dt)
        a_diag = -jnp.exp(A_log)

        def step(h, inp):
            dt_t, b_t, c_t, x_t = inp
            a_bar = jnp.exp(dt_t[:, :, None] * a_diag)
            h = a_bar * h + (dt_t * x_t)[:, :, None] * b_t[:, None, :]
            y = jnp.einsum('bds,bs->bd', h, c_t) + D * x_t
            return (h, y)
        h0 = jnp.zeros((Bb, D_INNER, D_STATE), dtype=x.dtype)
        _, ys = jax.lax.scan(step, h0, (dt.transpose(1, 0, 2), b_sel.transpose(1, 0, 2), c_sel.transpose(1, 0, 2), xs.transpose(1, 0, 2)))
        y = ys.transpose(1, 0, 2)
        return y * jax.nn.silu(z) @ W_out.T

    def _L0_ffn_ref(x, W1, b1, W2, b2, Wr, br):
        import jax, jax.numpy as jnp
        import numpy as np
        E = 8
        K = 2
        D = 128
        P = 512
        B, S, _ = x.shape
        xf = x.reshape(B * S, D)
        scores = xf @ Wr + br
        _, top_idx = jax.lax.top_k(scores, K)
        mask = jax.nn.one_hot(top_idx, E, dtype=scores.dtype).sum(-2) > 0
        router_weights = jax.nn.softmax(jnp.where(mask, scores, -jnp.inf), axis=-1)
        h = jax.nn.gelu(jnp.einsum('td,edp->etp', xf, W1) + b1[:, None, :])
        y = jnp.einsum('etp,epd->etd', h, W2) + b2[:, None, :]
        out = jnp.einsum('te,etd->td', router_weights, y)
        return out.reshape(B, S, D)
    x = L0_attn_x
    x = _layernorm(x + _L0_attn_ref(x, L0_attn_W_in, L0_attn_conv_w, L0_attn_conv_b, L0_attn_A_log, L0_attn_D, L0_attn_W_x, L0_attn_W_dt, L0_attn_b_dt, L0_attn_W_out), axis=-1)
    x = _layernorm(x + _L0_ffn_ref(x, L0_ffn_W1, L0_ffn_b1, L0_ffn_W2, L0_ffn_b2, L0_ffn_Wr, L0_ffn_br), axis=-1)
    return x

_drawn_inputs = setup_inputs


def setup_inputs(seed=0):
    import zlib

    import numpy as np

    out = dict(_drawn_inputs(seed))
    spreads = {'L0_attn_D': (1.0, 0.2)}
    factors = {'L0_attn_b_dt': 64.0,
     'L0_ffn_b1': 8.0,
     'L0_ffn_b2': 8.0,
     'L0_attn_W_x': 8.0,
     'L0_attn_W_dt': 8.0,
     'L0_attn_A_log': 8.0}
    for name, (base, spread) in spreads.items():
        noise = np.random.default_rng([zlib.crc32(name.encode()), seed]).standard_normal(out[name].shape)
        drawn = base * np.exp(spread * noise) if base else spread * noise
        out[name] = jnp.asarray(drawn.astype(out[name].dtype))
    for name, factor in factors.items():
        out[name] = (out[name] * factor).astype(out[name].dtype)
    return out
```

```python
from contextlib import ExitStack

import concourse.bass as bass
from concourse import mybir

F32 = mybir.dt.float32
F32R = mybir.dt.float32r
U8 = mybir.dt.uint8
ALU = mybir.AluOpType
ACT = mybir.ActivationFunctionType
AX_X = mybir.AxisListType.X

P = 128
EPS = 1e-5
LOG1P_SMALL = 2.0 ** -8
EXP_LN = "natural_log_exp_and_others"


class Unit:

    def __init__(self, pair, off):
        self.pair, self.off, self.par = pair, off, off % 2

    def shift(self, n):
        return Unit(self.pair, self.off + n)

    def at(self, per_unit, plus):
        return self.pair * (2 * per_unit) + (self.off * per_unit + plus)

    def half_at(self, per_pair, plus):
        return self.pair * per_pair + ((self.off // 2) * per_pair + plus)


class Has:

    def __init__(self, k, units):
        self.front = k + 1 < units
        self.scan = k < units
        self.next_scan = k + 1 < units
        self.ffn = 1 <= k <= units
        self.back = k < units
        self.ln2 = 2 <= k
        self.first = k == 0
        self.ffn_first = k == 1
        self.k = k


def mamba_moe_layer(nc, x, W_in, conv_w, conv_b, A_log, D, W_x, W_dt, b_dt, W_out, W1, b1, W2, b2, Wr, br, out):
    NB, L, DM = x.shape
    DI = W_out.shape[1]
    NS = A_log.shape[0]
    RK = W_dt.shape[1]
    TAPS = conv_w.shape[1]
    NE, _, PF = W1.shape
    TB = 512
    NT = TB // P
    NU = NB * L // TB
    DH = DI // P
    NC = PF // P
    HALO = TAPS - 1
    GROUPS = 4
    EG = NE // GROUPS
    GC = EG * NC
    ABARS = 8
    assert DM == P and DH == 2 and L == 2 * TB and NS == 16 and NU % 2 == 0 and RK + 4 * NS == P
    assert NE == 8 and NC == 4 and TAPS == 4

    ctx = ExitStack()

    def sb(name, shape, dt=F32):
        return ctx.enter_context(nc.sbuf_tensor(name, shape, dt))

    def ps(name, shape):
        return ctx.enter_context(nc.psum_tensor(name, shape, F32))

    def sem(name):
        return ctx.enter_context(nc.semaphore(name))

    with ctx:
        ident = sb("ident", [P, P])
        w1_hi = sb("w1_hi", [P, NE, PF], F32R)
        w1_lo = sb("w1_lo", [P, NE, PF], F32R)
        w2 = sb("w2", [P, NE, NC, DM])
        wconv_hi = sb("wconv_hi", [P, DH * TAPS, P], F32R)
        wconv_lo = sb("wconv_lo", [P, DH * TAPS, P], F32R)
        wz_hi = sb("wz_hi", [P, DH, P], F32R)
        wz_lo = sb("wz_lo", [P, DH, P], F32R)
        wx_t = sb("wx_t", [P, DH, P])
        wdt_t = sb("wdt_t", [RK, DI])
        wout_t = sb("wout_t", [P, DH, DM])
        NV = NE * NC + 3 * DH + NE
        vec_t = sb("vec_t", [P, NV])
        b1_t = vec_t[:, 0:NE * NC]
        conv_b_sb, d_sb, bdt_sb = (vec_t[:, NE * NC + DH * i:NE * NC + DH * (i + 1)] for i in range(3))
        b2_t = vec_t[:, NV - NE:NV]
        wr = sb("wr", [P, NE])
        wr_hi = sb("wr_hi", [P, NE], F32R)
        wr_lo = sb("wr_lo", [P, NE], F32R)
        br_all = sb("br_all", [P, NE])
        conv_w_sb = sb("conv_w_sb", [P, DH, TAPS])
        alog_all = sb("alog_all", [P, NS])
        a_exp = sb("a_exp", [P, NS])
        a_neg = sb("a_neg", [P, NS])
        select = sb("select", [P, 2 * NS], F32R)
        not_first = sb("not_first", [P, NT, NE])
        unread = sb("unread", [P, 4])
        minus_half = sb("minus_half", [P, NT])

        x_tok = sb("x_tok", [P, NT, DM])
        xt_hi = sb("xt_hi", [P, HALO + TB + 1], F32R)
        xt_lo = sb("xt_lo", [P, HALO + TB + 1], F32R)
        xs = sb("xs", [P, DH, TB])
        gate = [sb(f"gate{i}", [P, DH, TB]) for i in range(2)]
        bc_parts = [sb(f"bc_parts{i}", [P, TB], F32R) for i in range(2)]
        exp_v = sb("exp_v", [P, DH, TB])
        log_v = sb("log_v", [P, DH, TB])
        small_v = sb("small_v", [P, DH, TB])
        dt_rank = small_v[0:RK, 0, :]
        is_small = sb("is_small", [P, DH, TB], U8)
        dt = sb("dt", [P, DH, TB])
        u = [sb(f"u{i}", [P, DH, TB]) for i in range(2)]
        acc = [sb(f"acc{i}", [P, DH, TB]) for i in range(2)]
        carry = sb("carry", [P, NS, DH])
        x1 = [sb(f"x1_{i}", [P, NT, DM]) for i in range(2)]
        x1t_hi = sb("x1t_hi", [P, TB], F32R)
        x1t_lo = sb("x1t_lo", [P, TB], F32R)
        ln = [{n: sb(f"{n}{i}", s) for n, s in (("stats", [P, NT, 6]), ("meanvar", [P, NT, 2]), ("vareps", [P, NT]),
                                               ("rstd", [P, NT]))} for i in range(2)]
        score = sb("score", [P, NT, NE])
        top8 = sb("top8", [P, NT, 8])
        above = sb("above", [P, NT, NE])
        equal = sb("equal", [P, NT, NE])
        rank = sb("rank", [P, NT, NE])
        n_above = sb("n_above", [P, NT])
        room = sb("room", [P, NT])
        chosen = sb("chosen", [P, NT, NE])
        shifted = sb("shifted", [P, NT, NE])
        escore = sb("escore", [P, NT, NE])
        emask = sb("emask", [P, NT, NE])
        esum = sb("esum", [P, NT])
        einv = sb("einv", [P, NT])
        route = sb("route", [P, NT, NE])

        abar = [sb(f"abar{i}", [P, DH, TB]) for i in range(ABARS)]
        drive = [sb(f"drive{i}", [P, DH, TB]) for i in range(2)]
        h = [sb(f"h{i}", [P, DH, TB]) for i in range(2)]
        hc = [sb(f"hc{i}", [P, DH, TB]) for i in range(2)]
        hidden = sb("hidden", [P, GC, TB])
        weighted = sb("weighted", [P, TB])
        total = sb("total", [P, TB])
        weight = [sb(f"weight{i}", [P, TB]) for i in range(2)]

        w1_raw = hidden[:].rearrange("p a b -> p (a b)").rearrange("p (e f) -> p e f", e=NE)
        tap_w = abar[7][:].rearrange("p a b -> p (a b)").rearrange("p (n c) -> p n c", n=DH * TAPS)
        w_in_raw = abar[6][:, 0, :].rearrange("p (n c) -> p n c", c=DM)
        w_misc = abar[5][:].rearrange("p a b -> p (a b)")
        wx_raw, wout_raw = w_misc[0:RK + 2 * NS, 0:DI], w_misc[:, DI:2 * DI]
        wdt_raw = w_misc[:, 2 * DI:2 * DI + DH * RK].rearrange("p (h r) -> p h r", h=DH)
        vec_raw = w_misc[0:NV, 3 * DI:3 * DI + P]

        b_bank = [ps(f"b_bank{i}", [P, TB]) for i in range(2)]
        c_bank = [ps(f"c_bank{i}", [P, TB]) for i in range(2)]
        wide = [ps(f"wide{i}", [P, TB]) for i in range(2)]
        y = [ps(f"y{i}", [P, TB]) for i in range(2)]
        score_bank, sum_bank, turn_bank, route_bank, xdbl_bank, attn_bank = y[0], y[0], y[1], y[1], y[0], y[0]
        x1t_bank = wide[0]
        route_rows = weighted[0:NE, :]
        route_dram = nc.dram_tensor("route_scratch", (2, NE, TB), F32, kind="Internal").ap()

        w_in_in, w_misc_in, conv_w_in, small_in = sem("w_in_in"), sem("w_misc_in"), sem("conv_w_in"), sem("small_in")
        w1_in, w2_in = sem("w1_in"), sem("w2_in")
        x_in = sem("x_in")
        residual_in = [sem(f"residual_in{i}") for i in range(2)]
        out_done = [sem(f"out_done{i}") for i in range(2)]
        pool_setup, tap_w_done = sem("pool_setup"), sem("tap_w_done")
        setup_t = sem("setup_t")
        act_setup, dve_setup = sem("act_setup"), sem("dve_setup")
        xt_ready, xt_hi_done, xt_lo_done = sem("xt_ready"), sem("xt_hi_done"), sem("xt_lo_done")
        halo_hi, halo_lo = sem("halo_hi"), sem("halo_lo")
        inproj_ready, silu_done = sem("inproj_ready"), sem("silu_done")
        xdbl_ready, xdbl_act, bc_ready = sem("xdbl_ready"), sem("xdbl_act"), sem("bc_ready")
        v_ready, v_taken, e_ready, log_ready = sem("v_ready"), sem("v_taken"), sem("e_ready"), sem("log_ready")
        square_ready, poly_step, mask_done, log_fixed, dt_ready = sem("square_ready"), sem("poly_step"), sem("mask_done"), sem("log_fixed"), sem("dt_ready")
        u_ready, dx_ready = sem("u_ready"), sem("dx_ready")
        b_ready, c_ready = sem("b_ready"), sem("c_ready")
        abar_ready, drive_done, scan_done, hc_done, added = (
            sem("abar_ready"), sem("drive_done"), sem("scan_done"), sem("hc_done"), sem("added"))
        gated, attn_ready, res_done = sem("gated"), sem("attn_ready"), sem("res_done")
        route_turned, route_out, route_stored = sem("route_turned"), sem("route_out"), sem("route_stored")
        weight_in = [sem(f"weight_in{i}") for i in range(2)]
        sum_turned, sum_taken = sem("sum_turned"), sem("sum_taken")
        ln1_step, ln1_pow, ln1_done = sem("ln1_step"), sem("ln1_pow"), sem("ln1_done")
        ln2_step, ln2_pow, ln2_done = sem("ln2_step"), sem("ln2_pow"), sem("ln2_done")
        x1t_ready, x1t_hi_done, x1t_lo_done = sem("x1t_ready"), sem("x1t_hi_done"), sem("x1t_lo_done")
        score_ready, score_taken = sem("score_ready"), sem("score_taken")
        router_step, router_exp, route_step = sem("router_step"), sem("router_exp"), sem("route_step")
        w1_ready, gelu_done, y_ready, y_taken, ffn_added = (
            sem("w1_ready"), sem("gelu_done"), sem("y_ready"), sem("y_taken"), sem("ffn_added"))

        x_units = x.rearrange("b (h t p) c -> (b h) p t c", h=2, p=P)
        out_units = out.rearrange("b (h t p) c -> (b h) p t c", h=2, p=P)

        def both(bank):
            return bank[:].unsqueeze(1).to_broadcast([P, DH, TB])

        def bodies(engine, body):
            body(Unit(0, 0), Has(0, NU))
            body(Unit(0, 1), Has(1, NU))
            with engine.Fori(1, NU // 2 - 1) as pair:
                body(Unit(pair, 0), Has(2, NU))
                body(Unit(pair, 1), Has(3, NU))
            for k in range(NU - 2, NU + 2):
                body(Unit(k // 2, k % 2), Has(k, NU))

        def wait_apart(dve, semaphore, value, place):
            dve.wait_ge(semaphore, value)
            dve.memset(unread[:, place:place + 1], 0.0)

        def state_of(U, q):
            return (U, q + 4) if q + 4 < NS else (U.shift(1), q + 4 - NS)

        AFTER_SCAN = {5: 0, 7: 1, 9: 2, 11: 4, 15: 6}
        AFTER_C = {11: 3, 13: 5}
        WEIGHED = {**AFTER_SCAN, **{q - 1: e for q, e in AFTER_C.items()}}

        block = ctx.enter_context(nc.Block())

        @block.sync
        def _(sp):
            sp.dma_start(w_in_raw, W_in.rearrange("(n p) c -> p n c", p=P)).then_inc(w_in_in, 16)
            sp.dma_start(x_tok[:], x_units[0]).then_inc(x_in, 16)
            sp.dma_start(wx_raw, W_x).then_inc(w_misc_in, 16)
            sp.dma_start(wout_raw, W_out).then_inc(w_misc_in, 16)
            sp.dma_start(wdt_raw, W_dt.rearrange("(h p) r -> p h r", p=P)).then_inc(w_misc_in, 16)
            sp.dma_start(vec_raw[0:NE * NC], b1.rearrange("e (c p) -> (e c) p", p=P)).then_inc(w_misc_in, 16)
            sp.dma_start(vec_raw[NV - NE:NV], b2).then_inc(w_misc_in, 16)
            for i, v in enumerate((conv_b, D, b_dt)):
                at = NE * NC + DH * i
                sp.dma_start(vec_raw[at:at + DH], v.rearrange("(h p) -> h p", p=P)).then_inc(w_misc_in, 16)
            sp.dma_start(w1_raw, W1.rearrange("e d f -> d e f")).then_inc(w1_in, 16)
            sp.dma_start(w2[:], W2.rearrange("e (c p) d -> p e c d", p=P)).then_inc(w2_in, 16)
            sp.wait_ge(xt_ready, 1)
            sp.dma_start(x_tok[:], x_units[1]).then_inc(x_in, 16)

            def body(U, has):
                V, W = U.shift(-1), U.shift(-2)

                def weights_to_all(*experts):
                    for e in experts:
                        if e > 1:
                            sp.wait_ge(y_taken, V.at(NE, e - 1))
                        sp.dma_start(weight[e % 2][:], route_dram[V.par, e].partition_broadcast(P)).then_inc(
                            weight_in[e % 2], 16)

                if has.k + 2 < NU:
                    sp.wait_ge(xt_ready, U.at(1, 2))
                    sp.dma_start(x_tok[:], x_units[U.at(1, 2)]).then_inc(x_in, 16)
                if has.ffn:
                    sp.wait_ge(route_out, V.at(1, 1))
                    sp.dma_start(route_dram[V.par], route_rows).then_inc(route_stored, 16)
                    sp.wait_ge(route_stored, V.at(16, 16))
                    weights_to_all(0, 1)
                if has.ln2:
                    sp.wait_ge(ln2_done, W.at(1, 1))
                    sp.dma_start(out_units[W.at(1, 0)], x1[W.par][:]).then_inc(out_done[W.par], 16)
                if has.ffn:
                    weights_to_all(2, 3)
                if has.back:
                    if has.ln2:
                        sp.wait_ge(out_done[U.par], U.half_at(16, 0))
                    sp.dma_start(x1[U.par][:], x_units[U.at(1, 0)]).then_inc(residual_in[U.par], 16)
                if has.ffn:
                    weights_to_all(4, 5, 6, 7)

            bodies(sp, body)
            for i in range(2):
                sp.wait_ge(out_done[i], 16 * (NU // 2))

        @block.gpsimd
        def _(pool):
            pool.memset(ident[:], 0.0).then_inc(pool_setup, 1)
            pool.wait_ge(pool_setup, 1)
            pool.affine_select(out=ident[:], in_=ident[:], compare_op=ALU.not_equal, fill=1.0, base=0,
                               pattern=[[-1, P]], channel_multiplier=1).then_inc(pool_setup, 1)
            pool.memset(not_first[:], 1.0).then_inc(pool_setup, 1)
            pool.wait_ge(pool_setup, 3)
            pool.memset(not_first[:, :, 0:1], 0.0).then_inc(pool_setup, 1)
            pool.memset(minus_half[:], -0.5).then_inc(pool_setup, 1)

            def add_state(U, s, first_unit, last):
                pool.wait_ge(hc_done, U.at(NS, s + 1))
                if not last:
                    pool.wait_ge(scan_done, U.at(NS, s + 2))
                if s == 0:
                    pool.wait_ge(dx_ready, U.at(1, 1))
                if not (first_unit and s == 0):
                    pool.wait_ge(added, U.at(NS, s))
                pool.tensor_tensor(acc[U.par][:], acc[U.par][:], hc[s % 2][:], ALU.add).then_inc(added, 1)

            def add_expert(V, e):
                pool.wait_ge(y_taken, V.at(NE, e + 1))
                if e > 1:
                    pool.wait_ge(ffn_added, V.at(NE - 1, e - 1))
                pool.tensor_tensor(total[:], total[:], weighted[:], ALU.add).then_inc(ffn_added, 1)

            def power(U, which, step, done):
                pool.wait_ge(step, U.at(9, 9))
                pool.tensor_tensor(ln[which]["rstd"][:], ln[which]["vareps"][:], minus_half[:],
                                   ALU.pow).then_inc(done, 1)

            def log_poly(N, k):
                pool.wait_ge(square_ready, N.at(1, 1))
                pool.tensor_tensor(small_v[:], exp_v[:], small_v[:], ALU.subtract).then_inc(poly_step, 1)

            def dt_sum(N):
                pool.wait_ge(log_fixed, N.at(1, 1))
                pool.tensor_tensor(dt[:], dt[:], log_v[:], ALU.add).then_inc(dt_ready, 1)

            def dt_x(N, k):
                pool.wait_ge(dt_ready, N.at(1, 1))
                if k > 1:
                    pool.wait_ge(drive_done, N.at(NS, -NS))
                pool.tensor_tensor(u[N.par][:], dt[:], xs[:], ALU.mult).then_inc(u_ready, 1)

            for s in range(3):
                add_state(Unit(0, 0), s, True, False)

            def body(U, has):
                V, W, N = U.shift(-1), U.shift(-2), U.shift(1)
                for q in range(NS):
                    S, s = state_of(U, q - 1)
                    if (has.scan if q - 1 < NS - 4 else has.next_scan):
                        add_state(S, s, has.k == 0 and q - 1 < NS - 4, s == NS - 1)
                    if q == 0 and has.ln2:
                        add_expert(W, NE - 1)
                    if q == 1 and has.ln2:
                        power(W, 1, ln2_step, ln2_pow)
                    if has.ffn and WEIGHED.get(q):
                        add_expert(V, WEIGHED[q])
                    if q == 6 and has.front:
                        log_poly(N, has.k + 1)
                    if q == 8 and has.front:
                        dt_sum(N)
                        dt_x(N, has.k + 1)
                    if q == 13 and has.back:
                        power(U, 0, ln1_step, ln1_pow)

            bodies(pool, body)

        @block.scalar
        def _(act):
            act.dma_start(conv_w_sb[:], conv_w.rearrange("(h p) k -> p h k", p=P)).then_inc(conv_w_in, 16)
            act.dma_start(alog_all[:], A_log.partition_broadcast(P)).then_inc(small_in, 16)
            act.dma_start(wr[:], Wr).then_inc(small_in, 16)
            act.dma_start(br_all[:], br.partition_broadcast(P)).then_inc(small_in, 16)

            act.preload_act_table_set(EXP_LN)

            def x_hi(N, k):
                if k > 0:
                    act.wait_ge(inproj_ready, N.at(4, 0))
                if N.par:
                    act.copy(xt_hi[:, 0:HALO], xt_hi[:, TB:TB + HALO].bitcast(F32)).then_inc(halo_hi, 1)
                    act.wait_ge(halo_hi, N.at(1, 1))
                else:
                    act.mul(xt_hi[:, 0:HALO], ident[:, 0:HALO], 0.0).then_inc(halo_hi, 1)
                act.wait_ge(xt_ready, N.at(1, 1))
                act.copy(xt_hi[:, HALO:HALO + TB], turn_bank[:]).then_inc(xt_hi_done, 1)

            def xdbl_out(N, k):
                act.wait_ge(xdbl_ready, N.at(1, 1))
                if k > 1:
                    act.wait_ge(c_ready, N.at(NS, -NS))
                act.copy(bc_parts[N.par][64:P, :], xdbl_bank[64:P, :])
                if k > 0:
                    act.wait_ge(v_ready, N.at(2, 0))
                    act.wait_ge(log_fixed, N.at(1, 0))
                act.copy(dt_rank, xdbl_bank[0:RK, :]).then_inc(xdbl_act, 1)

            def silus(N, k):
                act.preload_act_table(ACT.Silu)
                for i in range(2 * DH):
                    if i == DH:
                        xdbl_out(N, k)
                    act.wait_ge(inproj_ready, N.at(4, i + 1))
                    if i < DH:
                        if i == 0 and k > 0:
                            act.wait_ge(u_ready, N.at(1, 0))
                        act.activation(xs[:, i, :], wide[i % 2][:], ACT.Silu,
                                       bias=conv_b_sb[:, i:i + 1]).then_inc(silu_done, 1)
                    else:
                        if i == DH and k > 1:
                            act.wait_ge(gated, N.at(1, -1))
                        act.activation(gate[N.par][:, i - DH, :], wide[i % 2][:], ACT.Silu).then_inc(silu_done, 1)

            def softplus_parts(N, k):
                if k > 0:
                    act.wait_ge(log_fixed, N.at(1, 0))
                    act.wait_ge(poly_step, N.at(1, 0))
                    act.wait_ge(u_ready, N.at(1, 0))
                    act.wait_ge(abar_ready, N.at(NS, 0))
                for i in range(DH):
                    act.wait_ge(v_ready, N.at(2, i + 1))
                    act.activation(exp_v[:, i, :], wide[i][:], ACT.Abs, bias=bdt_sb[:, i:i + 1]).then_inc(v_taken, 1)
                    act.activation(dt[:, i, :], wide[i][:], ACT.Relu, bias=bdt_sb[:, i:i + 1]).then_inc(v_taken, 1)
                act.wait_ge(v_taken, N.at(4, 4))
                act.activation(exp_v[:], exp_v[:], ACT.Exp, scale=-1.0).then_inc(e_ready, 1)
                act.wait_ge(e_ready, N.at(1, 1))
                act.activation(small_v[:], exp_v[:], ACT.Square, scale=0.5 ** 0.5).then_inc(square_ready, 1)
                act.activation(log_v[:], exp_v[:], ACT.Ln, bias=1.0).then_inc(log_ready, 1)

            def d_x(N, k):
                if k > 1:
                    act.wait_ge(gated, N.at(1, -1))
                    act.wait_ge(attn_ready, N.at(1, -1))
                act.wait_ge(silu_done, N.at(4, 2))
                for i in range(DH):
                    ins = act.mul(acc[N.par][:, i, :], xs[:, i, :], d_sb[:, i:i + 1])
                ins.then_inc(dx_ready, 1)

            def exps(S, states, first_unit):
                for s in states:
                    act.wait_ge(dt_ready, S.at(1, 1))
                    if not (first_unit and s < ABARS):
                        act.wait_ge(scan_done, S.at(NS, s + 1 - ABARS))
                    act.activation(abar[s % ABARS][:], dt[:], ACT.Exp,
                                   scale=a_neg[:, s:s + 1]).then_inc(abar_ready, 1)

            def gelus(V, g, first_unit, chunks=range(GC)):
                if g != 2 and chunks[0] == 0:
                    act.preload_act_table(ACT.Gelu_apprx_tanh)
                for c in chunks:
                    act.wait_ge(w1_ready, V.at(NE * NC, GC * g + c + 1))
                    if not (first_unit and g == 0):
                        act.wait_ge(y_ready, V.at(NE, EG * g - 1 + c // NC))
                    act.activation(hidden[:, c, :], wide[c % 2][:], ACT.Gelu_apprx_tanh,
                                   bias=b1_t[:, GC * g + c:GC * g + c + 1]).then_inc(gelu_done, 1)

            U0 = Unit(0, 0)
            act.wait_ge(pool_setup, 5)
            x_hi(U0, 0)
            act.wait_ge(small_in, 16 * 3)
            act.activation(a_exp[:], alog_all[:], ACT.Exp).then_inc(act_setup, 1)
            act.copy(wr_hi[:], wr[:]).then_inc(act_setup, 1)
            act.wait_ge(setup_t, 1)
            for h_ in range(DH):
                act.copy(wconv_hi[:, 4 * h_:4 * h_ + 4, :].rearrange("p n c -> p (n c)"), wide[h_][:])
            act.copy(wz_hi[:].rearrange("p n c -> p (n c)"), y[0][:, 0:2 * P]).then_inc(act_setup, 1)
            act.preload_act_table(ACT.Silu)
            act.wait_ge(dve_setup, 3)
            silus(U0, 0)
            act.preload_act_table_set(EXP_LN)
            softplus_parts(U0, 0)
            d_x(U0, 0)
            exps(U0, range(8), True)

            def body(U, has):
                V, N = U.shift(-1), U.shift(1)
                if has.ffn:
                    gelus(V, 0, has.ffn_first, range(7))
                if has.front:
                    x_hi(N, has.k + 1)
                if has.ffn:
                    gelus(V, 0, has.ffn_first, range(7, GC))
                if has.ffn or has.scan:
                    act.preload_act_table_set(EXP_LN)
                if has.ffn:
                    act.wait_ge(router_step, V.at(14, 5))
                    act.activation(escore[:], shifted[:], ACT.Exp).then_inc(router_exp, 1)
                if has.scan:
                    exps(U, range(8, 12), False)
                if has.first:
                    act.wait_ge(w1_in, 16)
                    act.copy(w1_hi[:], w1_raw).then_inc(act_setup, 1)
                if has.front:
                    silus(N, has.k + 1)
                if has.scan:
                    act.preload_act_table_set(EXP_LN)
                    exps(U, range(12, 16), False)
                if has.front:
                    softplus_parts(N, has.k + 1)
                if has.ffn:
                    gelus(V, 1, False)
                if has.front:
                    d_x(N, has.k + 1)
                if has.ffn:
                    gelus(V, 2, False)
                if has.next_scan:
                    act.preload_act_table_set(EXP_LN)
                    exps(N, range(0, 4), False)
                if has.ffn:
                    gelus(V, 3, False)
                if has.next_scan:
                    act.preload_act_table_set(EXP_LN)
                    exps(N, range(4, 6), False)
                if has.back:
                    act.wait_ge(x1t_ready, U.at(1, 1))
                    if not has.first:
                        act.wait_ge(score_taken, U.at(1, 0))
                        act.wait_ge(w1_ready, U.at(NE * NC, 0))
                    act.copy(x1t_hi[:], x1t_bank[:]).then_inc(x1t_hi_done, 1)
                if has.next_scan:
                    exps(N, range(6, 8), False)

            bodies(act, body)

        @block.vector
        def _(dve):
            dve.wait_ge(w_in_in, 16)
            dve.wait_ge(conv_w_in, 16)
            for n in range(DH * TAPS):
                ins = dve.tensor_scalar(tap_w[:, n, :], w_in_raw[:, n // TAPS, :],
                                        conv_w_sb[:, n // TAPS, n % TAPS:n % TAPS + 1], None, ALU.mult)
            ins.then_inc(tap_w_done, 1)
            dve.wait_ge(act_setup, 2)
            dve.tensor_scalar(a_neg[:], a_exp[:], -1.0, None, ALU.mult)
            dve.tensor_tensor(wr_lo[:], wr[:], wr_hi[:].bitcast(F32), ALU.subtract)
            dve.wait_ge(pool_setup, 5)
            dve.tensor_tensor(select[:], ident[:, 64:64 + 2 * NS], ident[:, 96:96 + 2 * NS],
                              ALU.add).then_inc(dve_setup, 1)
            def x_lo(N, k):
                if k > 0:
                    dve.wait_ge(inproj_ready, N.at(4, 0))
                if N.par:
                    dve.tensor_copy(xt_lo[:, 0:HALO], xt_lo[:, TB:TB + HALO].bitcast(F32)).then_inc(halo_lo, 1)
                    dve.wait_ge(halo_lo, N.at(1, 1))
                else:
                    dve.tensor_scalar(xt_lo[:, 0:HALO], ident[:, 0:HALO], 0.0, None, ALU.mult).then_inc(halo_lo, 1)
                dve.wait_ge(xt_hi_done, N.at(1, 1))
                dve.tensor_tensor(xt_lo[:, HALO:HALO + TB], turn_bank[:], xt_hi[:, HALO:HALO + TB].bitcast(F32),
                                  ALU.subtract).then_inc(xt_lo_done, 1)

            def bc_lo(N):
                dve.wait_ge(xdbl_act, N.at(1, 1))
                lo = bc_parts[N.par][96:P, :]
                dve.tensor_tensor(lo, xdbl_bank[96:P, :], lo.bitcast(F32), ALU.subtract).then_inc(bc_ready, 1)

            def log_fix(N, k):
                dve.wait_ge(e_ready, N.at(1, 1))
                if k > 0:
                    dve.wait_ge(log_fixed, N.at(1, 0))
                dve.tensor_scalar(is_small[:], exp_v[:], LOG1P_SMALL, None, ALU.is_lt).then_inc(mask_done, 1)
                dve.wait_ge(mask_done, N.at(1, 1))
                dve.wait_ge(log_ready, N.at(1, 1))
                wait_apart(dve, poly_step, N.at(1, 1), 2)
                dve.copy_predicated(log_v[:], is_small[:], small_v[:]).then_inc(log_fixed, 1)

            def drive_in(S, s, k):
                dve.wait_ge(b_ready, S.at(NS, s + 1))
                if s == 0:
                    dve.wait_ge(u_ready, S.at(1, 1))
                if k > 0 or s > 1:
                    dve.wait_ge(scan_done, S.at(NS, s - 1))
                dve.tensor_tensor(drive[s % 2][:], u[S.par][:], both(b_bank[s % 2]), ALU.mult).then_inc(drive_done, 1)

            def scan(S, s, k):
                dve.wait_ge(drive_done, S.at(NS, s + 1))
                dve.wait_ge(abar_ready, S.at(NS, s + 1))
                if k > 0 or s > 1:
                    dve.wait_ge(hc_done, S.at(NS, s - 1))
                for i in range(DH):
                    start = carry[:, s, i:i + 1] if S.par else 0.0
                    ins = dve.tensor_tensor_scan(h[s % 2][:, i, :], abar[s % ABARS][:, i, :], drive[s % 2][:, i, :],
                                                 start, ALU.mult, ALU.add)
                ins.then_inc(scan_done, 1)

            def times_c(S, s, k):
                dve.wait_ge(scan_done, S.at(NS, s + 1))
                dve.wait_ge(c_ready, S.at(NS, s + 1))
                if k > 0 or s > 1:
                    dve.wait_ge(added, S.at(NS, s - 1))
                if not S.par:
                    dve.tensor_copy(carry[:, s, :], h[s % 2][:, :, TB - 1])
                dve.tensor_tensor(hc[s % 2][:], h[s % 2][:], both(c_bank[s % 2]), ALU.mult).then_inc(hc_done, 1)

            def statistics(U, which, step):
                t = ln[which]
                for i in range(NT):
                    dve.bn_stats(t["stats"][:, i, :], x1[U.par][:, i, :]).then_inc(step, 1)

            def mean_var(U, which, step):
                t = ln[which]
                wait_apart(dve, step, U.at(9, NT), which)
                for i in range(NT):
                    dve.bn_aggr(t["meanvar"][:, i, :], t["stats"][:, i, :]).then_inc(step, 1)
                dve.wait_ge(step, U.at(9, 8))
                dve.tensor_scalar(t["vareps"][:], t["meanvar"][:, :, 1], EPS, None, ALU.add).then_inc(step, 1)

            def normalise(U, which, powered, done):
                t = ln[which]
                dve.wait_ge(powered, U.at(1, 1))
                for i in range(NT):
                    ins = dve.tensor_scalar(x1[U.par][:, i, :], x1[U.par][:, i, :], t["meanvar"][:, i, 0:1],
                                            t["rstd"][:, i:i + 1], ALU.subtract, ALU.mult)
                ins.then_inc(done, 1)

            def gate_acc(U):
                dve.wait_ge(added, U.at(NS, NS))
                dve.wait_ge(silu_done, U.at(4, 4))
                dve.tensor_tensor(acc[U.par][:], acc[U.par][:], gate[U.par][:], ALU.mult).then_inc(gated, 1)

            def residual(U, k):
                dve.wait_ge(attn_ready, U.at(1, 1))
                dve.wait_ge(residual_in[U.par], U.half_at(16, 16))
                if k > 0:
                    dve.wait_ge(ln1_pow, U.at(1, 0))
                dve.tensor_tensor(x1[U.par][:], attn_bank[:].rearrange("p (t d) -> p t d", t=NT), x1[U.par][:],
                                  ALU.add).then_inc(res_done, 1)
                dve.wait_ge(res_done, U.at(1, 1))

            def x1_lo(U):
                dve.wait_ge(x1t_hi_done, U.at(1, 1))
                dve.tensor_tensor(x1t_lo[:], x1t_bank[:], x1t_hi[:].bitcast(F32), ALU.subtract).then_inc(x1t_lo_done, 1)

            def over_experts(col):
                return col.unsqueeze(2).to_broadcast([P, NT, NE])

            def step(V, n):
                dve.wait_ge(router_step, V.at(14, n))

            def router_score(V):
                dve.wait_ge(score_ready, V.at(1, 1))
                dve.tensor_tensor(score[:], score_bank[:, 0:NT * NE].rearrange("p (t e) -> p t e", t=NT),
                                  br_all[:].unsqueeze(1).to_broadcast([P, NT, NE]), ALU.add).then_inc(score_taken, 1)

            def router_max(V):
                wait_apart(dve, score_taken, V.at(1, 1), 3)
                for i in range(NT):
                    dve.max(top8[:, i, :], score[:, i, :]).then_inc(router_step, 1)

            def router_compare(V):
                step(V, 4)
                dve.tensor_tensor(shifted[:], score[:], over_experts(top8[:, :, 0]),
                                  ALU.subtract).then_inc(router_step, 1)
                second = over_experts(top8[:, :, 1])
                dve.tensor_tensor(above[:], score[:], second, ALU.is_gt).then_inc(router_step, 1)
                dve.tensor_tensor(equal[:], score[:], second, ALU.is_equal).then_inc(router_step, 1)

            def router_count(V):
                step(V, 7)
                dve.tensor_tensor_scan(rank[:].rearrange("p t e -> p (t e)"), not_first[:].rearrange("p t e -> p (t e)"),
                                       equal[:].rearrange("p t e -> p (t e)"), 0.0, ALU.mult,
                                       ALU.add).then_inc(router_step, 1)
                dve.tensor_reduce(n_above[:], above[:], AX_X, ALU.add).then_inc(router_step, 1)

            def router_room(V):
                step(V, 9)
                dve.tensor_scalar(room[:], n_above[:], -1.0, 2.0, ALU.mult, ALU.add).then_inc(router_step, 1)

            def router_fits(V):
                step(V, 10)
                dve.tensor_tensor(rank[:], rank[:], over_experts(room[:]), ALU.is_le).then_inc(router_step, 1)

            def router_equals(V):
                step(V, 11)
                dve.tensor_tensor(rank[:], rank[:], equal[:], ALU.mult).then_inc(router_step, 1)

            def router_chosen(V):
                step(V, 12)
                dve.tensor_tensor(chosen[:], rank[:], above[:], ALU.add).then_inc(router_step, 1)
                step(V, 13)
                dve.wait_ge(router_exp, V.at(1, 1))
                dve.tensor_tensor(emask[:], escore[:], chosen[:], ALU.mult).then_inc(router_step, 1)

            def router_sum(V):
                step(V, 14)
                dve.tensor_reduce(esum[:], emask[:], AX_X, ALU.add).then_inc(route_step, 1)

            def router_divide(V):
                dve.wait_ge(route_step, V.at(3, 1))
                dve.reciprocal(einv[:], esum[:]).then_inc(route_step, 1)
                dve.wait_ge(route_step, V.at(3, 2))
                dve.tensor_tensor(route[:], emask[:], over_experts(einv[:]), ALU.mult).then_inc(route_step, 1)

            def rows_of_route(V):
                dve.wait_ge(route_turned, V.at(1, 1))
                dve.wait_ge(route_step, V.at(3, 3))
                dve.tensor_copy(route_rows, route_bank[0:NE, :]).then_inc(route_out, 1)

            def weigh(V, e):
                dve.wait_ge(y_ready, V.at(NE, e + 1))
                dve.wait_ge(weight_in[e % 2], V.at(16 * NE // 2, 16 * (e // 2 + 1)))
                if e == 1:
                    dve.wait_ge(route_stored, V.at(16, 16))
                if e > 1:
                    dve.wait_ge(ffn_added, V.at(NE - 1, e - 1))
                dve.scalar_tensor_tensor(out=(weighted if e else total)[:], in0=y[e % 2][:], scalar=b2_t[:, e:e + 1],
                                         in1=weight[e % 2][:], op0=ALU.add, op1=ALU.mult).then_inc(y_taken, 1)

            def add_experts(W):
                dve.wait_ge(sum_turned, W.at(1, 1))
                dve.tensor_tensor(x1[W.par][:], sum_bank[:].rearrange("p (t d) -> p t d", t=NT), x1[W.par][:],
                                  ALU.add).then_inc(sum_taken, 1)

            U0 = Unit(0, 0)
            x_lo(U0, 0)
            dve.wait_ge(act_setup, 3)
            for h_ in range(DH):
                dve.tensor_tensor(wconv_lo[:, 4 * h_:4 * h_ + 4, :].rearrange("p n c -> p (n c)"), wide[h_][:],
                                  wconv_hi[:, 4 * h_:4 * h_ + 4, :].rearrange("p n c -> p (n c)").bitcast(F32),
                                  ALU.subtract)
            dve.tensor_tensor(wz_lo[:].rearrange("p n c -> p (n c)"), y[0][:, 0:2 * P],
                              wz_hi[:].rearrange("p n c -> p (n c)").bitcast(F32),
                              ALU.subtract).then_inc(dve_setup, 1)
            dve.wait_ge(setup_t, 2)
            dve.tensor_copy(wout_t[:].rearrange("p h d -> p (h d)"), c_bank[0][:, 0:2 * P])
            dve.tensor_copy(wdt_t[:], c_bank[0][0:RK, 2 * P:4 * P])
            NX = RK + 2 * NS
            wx_bank = b_bank[0][:, 0:2 * NX].rearrange("p (h n) -> p h n", h=DH)
            dve.tensor_copy(wx_t[:, :, 0:NX], wx_bank)
            dve.tensor_copy(wx_t[:, :, NX:P], wx_bank[:, :, RK:NX])
            dve.tensor_copy(vec_t[:], b_bank[0][:, 2 * NX:2 * NX + NV]).then_inc(dve_setup, 1)
            bc_lo(U0)
            dve.wait_ge(square_ready, 1)
            dve.tensor_tensor(small_v[:], exp_v[:], small_v[:], ALU.subtract).then_inc(poly_step, 1)
            log_fix(U0, 0)
            dve.wait_ge(log_fixed, 1)
            dve.tensor_tensor(dt[:], dt[:], log_v[:], ALU.add).then_inc(dt_ready, 1)
            dve.wait_ge(dt_ready, 1)
            dve.tensor_tensor(u[0][:], dt[:], xs[:], ALU.mult).then_inc(u_ready, 1)
            drive_in(U0, 0, 0)
            for s in range(4):
                if s:
                    times_c(U0, s - 1, 0)
                drive_in(U0, s + 1, 0)
                scan(U0, s, 0)

            def body(U, has):
                V, W, N = U.shift(-1), U.shift(-2), U.shift(1)

                def k_of(q):
                    return has.k if q < NS - 4 else has.k + 1

                for q in range(NS):
                    here = has.scan if q < NS - 4 else has.next_scan
                    before = has.scan if q - 1 < NS - 4 else has.next_scan
                    after = has.scan if q + 1 < NS - 4 else has.next_scan
                    if before:
                        times_c(*state_of(U, q - 1), k_of(q - 1))
                    if q in AFTER_C and has.ffn:
                        weigh(V, AFTER_C[q])
                    if q == 1 and has.ffn:
                        router_compare(V)
                    if q == 2 and has.ffn:
                        router_chosen(V)
                    if q == 4 and has.front:
                        bc_lo(N)
                    if q == 15 and has.back:
                        x1_lo(U)
                    if after:
                        drive_in(*state_of(U, q + 1), k_of(q + 1))
                    if q == 0 and has.ffn:
                        router_score(V)
                    if q == 1 and has.ffn:
                        router_count(V)
                    if q == 2 and has.ffn:
                        router_sum(V)
                    if q == 14 and has.back:
                        normalise(U, 0, ln1_pow, ln1_done)
                    if here:
                        scan(*state_of(U, q), k_of(q))
                    if has.first and q >= 4 and q - 4 < NE:
                        e = q - 4
                        dve.wait_ge(act_setup, 4)
                        dve.tensor_tensor(w1_lo[:, e, :], w1_raw[:, e, :], w1_hi[:, e, :].bitcast(F32),
                                          ALU.subtract).then_inc(dve_setup, 1)
                    if q == 0 and has.ln2:
                        weigh(W, NE - 1)
                    if q == 0 and has.ffn:
                        router_max(V)
                    if q == 1:
                        if has.ln2:
                            add_experts(W)
                        if has.ffn:
                            router_room(V)
                        if has.front:
                            x_lo(N, has.k + 1)
                        if has.ln2:
                            dve.wait_ge(sum_taken, W.at(1, 1))
                            statistics(W, 1, ln2_step)
                        if has.ffn:
                            router_fits(V)
                        if has.ln2:
                            mean_var(W, 1, ln2_step)
                        if has.ffn:
                            router_equals(V)
                    if q == 2 and has.ffn:
                        router_divide(V)
                    if q == 3 and has.ln2:
                        normalise(W, 1, ln2_pow, ln2_done)
                    if q == 3 and has.ffn:
                        rows_of_route(V)
                    if q in AFTER_SCAN and has.ffn:
                        weigh(V, AFTER_SCAN[q])
                    if q == 8 and has.front:
                        log_fix(N, has.k + 1)
                    if q == 12 and has.back:
                        gate_acc(U)
                    if q == 13 and has.back:
                        residual(U, has.k)
                        statistics(U, 0, ln1_step)
                        mean_var(U, 0, ln1_step)

            bodies(dve, body)

        @block.tensor
        def _(pe):
            pe.wait_ge(pool_setup, 5)
            pe.wait_ge(x_in, 16)
            for i in range(NT):
                ins = pe.transpose(turn_bank[:, i * P:(i + 1) * P], x_tok[:, i, :], ident[:])
            ins.then_inc(xt_ready, 1)
            pe.wait_ge(tap_w_done, 1)
            for n in range(DH * TAPS):
                pe.transpose(wide[n // TAPS][:, (n % TAPS) * P:(n % TAPS + 1) * P], tap_w[:, n, :], ident[:])
            for n in range(DH):
                ins = pe.transpose(y[0][:, n * P:(n + 1) * P], w_in_raw[:, DH + n, :], ident[:])
            ins.then_inc(setup_t, 1)
            pe.wait_ge(w_misc_in, 16 * 8)
            NX = RK + 2 * NS
            for n in range(DH):
                pe.transpose(c_bank[0][:, n * P:(n + 1) * P], wout_raw[:, n * P:(n + 1) * P], ident[:])
                pe.transpose(c_bank[0][0:RK, (DH + n) * P:(DH + n + 1) * P], wdt_raw[:, n, :], ident[:])
                pe.transpose(b_bank[0][:, n * NX:(n + 1) * NX], wx_raw[:, n * P:(n + 1) * P], ident[0:NX, 0:NX])
            pe.transpose(b_bank[0][:, 2 * NX:2 * NX + NV], vec_raw, ident[0:NV, 0:NV]).then_inc(setup_t, 1)

            def split_product(bank, w_hi, w_lo, x_hi, x_lo, start, stop):
                pe.matmul(bank, w_lo, x_hi, start=start, stop=False)
                pe.matmul(bank, w_hi, x_lo, start=False, stop=False)
                return pe.matmul(bank, w_hi, x_hi, start=False, stop=stop)

            def x_turn(N, k):
                pe.wait_ge(x_in, N.at(16, 16))
                if k > 2:
                    pe.wait_ge(y_taken, N.at(NE, -2 * NE))
                for i in range(NT):
                    ins = pe.transpose(turn_bank[:, i * P:(i + 1) * P], x_tok[:, i, :], ident[:])
                ins.then_inc(xt_ready, 1)

            def conv_half(N, i, k):
                pe.wait_ge(xt_lo_done, N.at(1, 1))
                for t in range(TAPS):
                    ins = split_product(wide[i][:], wconv_hi[:, i * TAPS + t, :], wconv_lo[:, i * TAPS + t, :],
                                        xt_hi[:, t:t + TB], xt_lo[:, t:t + TB], t == 0, t == TAPS - 1)
                ins.then_inc(inproj_ready, 1)

            def z_half(N, i):
                pe.wait_ge(silu_done, N.at(4, i + 1))
                split_product(wide[i][:], wz_hi[:, i, :], wz_lo[:, i, :], xt_hi[:, HALO:HALO + TB],
                              xt_lo[:, HALO:HALO + TB], True, True).then_inc(inproj_ready, 1)

            def x_dbl(N, ffn, ln2):
                pe.wait_ge(silu_done, N.at(4, 2))
                if ffn:
                    pe.wait_ge(score_taken, N.at(1, -1))
                if ln2:
                    pe.wait_ge(sum_taken, N.at(1, -2))
                for i in range(DH):
                    ins = pe.matmul(xdbl_bank[:], wx_t[:, i, :], xs[:, i, :], start=(i == 0), stop=(i == DH - 1))
                ins.then_inc(xdbl_ready, 1)

            def v_half(N, i):
                pe.wait_ge(xdbl_act, N.at(1, 1))
                pe.wait_ge(silu_done, N.at(4, 4))
                pe.matmul(wide[i][:], wdt_t[:, i * P:(i + 1) * P], dt_rank, start=True,
                          stop=True).then_inc(v_ready, 1)

            def broadcast(bank, parts, row):
                return pe.matmul(bank[:], select[64:P, row:row + 1].to_broadcast([64, P]), parts[64:P, :],
                                 start=True, stop=True)

            def b_row(S, s, k):
                if s == 0:
                    pe.wait_ge(bc_ready, S.at(1, 1))
                if k > 0 or s > 1:
                    pe.wait_ge(drive_done, S.at(NS, s - 1))
                broadcast(b_bank[s % 2], bc_parts[S.par], s).then_inc(b_ready, 1)

            def c_row(S, s, k):
                if k > 0 or s > 1:
                    pe.wait_ge(hc_done, S.at(NS, s - 1))
                broadcast(c_bank[s % 2], bc_parts[S.par], NS + s).then_inc(c_ready, 1)

            def first_layer(V, g, chunks, has):
                for c in chunks:
                    if c >= 2:
                        pe.wait_ge(gelu_done, V.at(NE * NC, GC * g + c - 1))
                    elif g > 0 or not has.ffn_first:
                        pe.wait_ge(gelu_done, V.at(NE * NC, GC * g + c - 1))
                    if g == 0 and c == 0:
                        pe.wait_ge(x1t_lo_done, V.at(1, 1))
                        if has.scan:
                            pe.wait_ge(v_taken, V.shift(1).at(4, 4))
                    if g == 1 and c == 0 and has.front:
                        pe.wait_ge(v_taken, V.shift(2).at(4, 4))
                    e, c4 = EG * g + c // NC, c % NC
                    w = slice(c4 * P, (c4 + 1) * P)
                    split_product(wide[c % 2][:], w1_hi[:, e, w], w1_lo[:, e, w], x1t_hi[:], x1t_lo[:], True,
                                  True).then_inc(w1_ready, 1)

            def second_layer(V, e, chunks, has):
                for c in chunks:
                    if c == 0:
                        if e >= 2:
                            pe.wait_ge(y_taken, V.at(NE, e - 1))
                        if e == 0 and has.ln2:
                            pe.wait_ge(sum_taken, V.at(1, 0))
                        if e == 0:
                            pe.wait_ge(score_taken, V.at(1, 1))
                        if e == 0 and has.front:
                            pe.wait_ge(bc_ready, V.at(1, 3))
                        if e == 1:
                            pe.wait_ge(route_out, V.at(1, 1))
                        if e == 6 and has.back:
                            pe.wait_ge(res_done, V.at(1, 2))
                    pe.wait_ge(gelu_done, V.at(NE * NC, NC * e + c + 1))
                    ins = pe.matmul(y[e % 2][:], w2[:, e, c, :], hidden[:, NC * (e % EG) + c, :],
                                    start=(c == 0), stop=(c == NC - 1), skip_group_check=True)
                if c == NC - 1:
                    ins.then_inc(y_ready, 1)

            def route_turn(V, has):
                pe.wait_ge(route_step, V.at(3, 3))
                if has.front:
                    pe.wait_ge(xt_lo_done, V.at(1, 3))
                for i in range(NT):
                    ins = pe.transpose(route_bank[0:NE, i * P:(i + 1) * P], route[:, i, :], ident[:])
                ins.then_inc(route_turned, 1)

            def sum_turn(W, has):
                pe.wait_ge(ffn_added, W.at(NE - 1, NE - 1))
                if has.ffn:
                    pe.wait_ge(score_taken, W.at(1, 2))
                for i in range(NT):
                    ins = pe.transpose(sum_bank[:, i * P:(i + 1) * P], total[:, i * P:(i + 1) * P], ident[:])
                ins.then_inc(sum_turned, 1)

            def out_projection(U, has):
                pe.wait_ge(gated, U.at(1, 1))
                if has.ffn:
                    pe.wait_ge(y_taken, U.at(NE, 5 - NE))
                elif has.front:
                    pe.wait_ge(bc_ready, U.at(1, 2))
                for i in range(NT):
                    for j in range(DH):
                        ins = pe.matmul(attn_bank[:, i * P:(i + 1) * P], acc[U.par][:, j, i * P:(i + 1) * P],
                                        wout_t[:, j, :], start=(j == 0), stop=(j == DH - 1))
                ins.then_inc(attn_ready, 1)

            def x1_turn(U, has):
                pe.wait_ge(ln1_done, U.at(1, 1))
                if has.ffn:
                    pe.wait_ge(gelu_done, U.at(NE * NC, 0))
                elif has.front:
                    pe.wait_ge(v_taken, U.at(4, 8))
                for i in range(NT):
                    ins = pe.transpose(x1t_bank[:, i * P:(i + 1) * P], x1[U.par][:, i, :], ident[:])
                ins.then_inc(x1t_ready, 1)

            def scores(V, ffn_before):
                pe.wait_ge(x1t_lo_done, V.at(1, 1))
                if ffn_before:
                    pe.wait_ge(y_taken, V.at(NE, -1))
                for i in range(NT):
                    t = slice(i * P, (i + 1) * P)
                    ins = split_product(score_bank[:, i * NE:(i + 1) * NE], x1t_hi[:, t], x1t_lo[:, t], wr_hi[:], wr_lo[:],
                                        True, True)
                ins.then_inc(score_ready, 1)

            U0 = Unit(0, 0)
            pe.wait_ge(dve_setup, 2)
            for i in range(DH):
                conv_half(U0, i, 0)
            pe.wait_ge(dve_setup, 3)
            x_dbl(U0, False, False)
            for i in range(DH):
                z_half(U0, i)
            for i in range(DH):
                v_half(U0, i)
            b_row(U0, 0, 0)
            b_row(U0, 1, 0)
            for s in range(4):
                b_row(U0, s + 2, 0)
                c_row(U0, s, 0)

            def body(U, has):
                V, N = U.shift(-1), U.shift(1)

                def layer1(g, *chunks):
                    if has.ffn:
                        first_layer(V, g, chunks, has)

                def layer2(e, *tiles):
                    if has.ffn:
                        second_layer(V, e, tiles, has)

                def rows(q):
                    if (has.scan if q + 2 < NS - 4 else has.next_scan):
                        b_row(*state_of(U, q + 2), has.k if q + 2 < NS - 4 else has.k + 1)
                    if (has.scan if q < NS - 4 else has.next_scan):
                        c_row(*state_of(U, q), has.k if q < NS - 4 else has.k + 1)

                if has.ffn and not has.scan:
                    scores(V, has.ln2)
                    layer1(0, 0, 1, 2, 3, 4, 5, 6, 7)
                    sum_turn(U.shift(-2), has)
                    layer2(0, 0, 1, 2, 3)
                    route_turn(V, has)
                    for e in range(1, NE - 1):
                        for c in range(NC):
                            layer1((e + 1) // EG, NC * ((e + 1) % EG) + c)
                            layer2(e, c)
                    layer2(NE - 1, 0, 1, 2, 3)
                    return
                if has.ffn_first:
                    pe.wait_ge(dve_setup, 3 + NE)
                    pe.wait_ge(w2_in, 16)
                rows(0)
                if has.ffn:
                    scores(V, has.ln2)
                layer1(0, 0, 1, 2, 3, 4)
                rows(1)
                layer1(0, *range(5, 7))
                if has.ln2:
                    sum_turn(U.shift(-2), has)
                if has.front:
                    x_turn(N, has.k + 1)
                layer1(0, *range(7, GC))
                rows(2)
                if has.front:
                    conv_bank_free(has, U, V)
                    conv_half(N, 0, has.k + 1)
                    conv_half(N, 1, has.k + 1)
                rows(3)
                if has.front:
                    z_half(N, 0)
                    x_dbl(N, has.ffn, has.ln2)
                    z_half(N, 1)
                if has.ffn:
                    route_turn(V, has)
                rows(4)
                if has.front:
                    v_half(N, 0)
                    v_half(N, 1)
                layer2(0, 0, 1, 2, 3)
                rows(5)
                layer2(1, 0, 1, 2, 3)
                layer1(1, 0)
                rows(6)
                layer1(1, 1)
                rows(7)
                layer1(1, 2, 3, 4, 5, 6, 7)
                layer2(2, 0)
                rows(8)
                layer2(2, 1, 2, 3)
                layer1(2, 0, 1)
                layer2(3, 0)
                rows(9)
                layer2(3, 1, 2, 3)
                layer1(2, 2, 3, 4)
                rows(10)
                layer1(2, 5, 6, 7)
                layer2(4, 0, 1, 2, 3)
                layer1(3, 0)
                rows(11)
                layer1(3, 1)
                layer2(5, 0, 1, 2)
                rows(12)
                layer2(5, 3)
                layer1(3, 2)
                rows(13)
                if has.back:
                    out_projection(U, has)
                layer1(3, 3, 4, 5)
                rows(14)
                layer1(3, 6, 7)
                layer2(6, 0, 1, 2)
                rows(15)
                if has.back:
                    x1_turn(U, has)
                layer2(6, 3)
                layer2(7, 0, 1, 2, 3)

            def conv_bank_free(has, U, V):
                if has.ffn:
                    pe.wait_ge(gelu_done, V.at(NE * NC, GC))
                else:
                    pe.wait_ge(v_taken, U.at(4, 4))

            bodies(pe, body)


_INS = ["L0_attn_x", "L0_attn_W_in", "L0_attn_conv_w", "L0_attn_conv_b", "L0_attn_A_log", "L0_attn_D", "L0_attn_W_x",
        "L0_attn_W_dt", "L0_attn_b_dt", "L0_attn_W_out", "L0_ffn_W1", "L0_ffn_b1", "L0_ffn_W2", "L0_ffn_b2",
        "L0_ffn_Wr", "L0_ffn_br"]


def kernel(**inputs):
    import numpy as _np
    import concourse.bacc as _bacc
    from concourse import mybir as _mybir
    from concourse.bass_utils import run_bass_kernel_spmd as _run

    nc = _bacc.Bacc("TRN2", target_bir_lowering=False, num_devices=1)
    arrays, args = {}, []
    for name in _INS:
        a = _np.ascontiguousarray(inputs[name])
        arrays[f"in_{name}"] = a
        args.append(nc.dram_tensor(f"in_{name}", a.shape, _mybir.dt.from_np(a.dtype), kind="ExternalInput").ap())
    shape = inputs["L0_attn_x"].shape
    args.append(nc.dram_tensor("out_0", shape, _mybir.dt.float32, kind="ExternalOutput").ap())
    mamba_moe_layer(nc, *args)
    r = _run(nc, [arrays], core_ids=[0])
    return r.results[0]["out_0"]
```
